# Optimizing a Trainium2 kernel written in Bass

```python
import numpy as np
import jax
import jax.numpy as jnp

def _softmax(x, axis=-1):
    return jax.nn.softmax(x, axis=axis)

def _gelu(x):
    return jax.nn.gelu(x, approximate=True)

def _silu(x):
    return jax.nn.silu(x)

def _sigmoid(x):
    return jax.nn.sigmoid(x)

def _layernorm(x, axis=-1, eps=1e-05):
    m = jnp.mean(x, axis=axis, keepdims=True)
    v = jnp.var(x, axis=axis, keepdims=True)
    return (x - m) / jnp.sqrt(v + eps)

def _scatter_add(tgt, idx, src, axis=0):
    return tgt.at[idx].add(src)

def _segment_sum(src, seg, n):
    return jax.ops.segment_sum(src, seg, n)
kernel_name = 'mk_dlrm_tower_d1_rec_r8_bd556e'

def setup_inputs(seed: int=0):
    np.random.seed(seed)
    _w = jnp.asarray

    def _rec_inputs():
        import jax
        import jax.numpy as jnp
        _tk = jax.random.key(seed)
        ids = jnp.stack([jax.random.randint(jax.random.fold_in(_tk, 200 + f), (512,), 0, v, jnp.int32) for f, v in enumerate([1250, 1000, 1250, 125000, 12500, 12500, 12500, 1250, 1000, 1000, 1000, 1250, 12500, 12500, 12500, 12500, 1250, 12500, 1000, 1000, 1000, 1250, 1000, 1250, 1250, 1000])], axis=1)
        tbl_0 = 0.05 * jax.random.normal(jax.random.fold_in(_tk, 500 + 0), (1250, 128), jnp.float32)
        tbl_1 = 0.05 * jax.random.normal(jax.random.fold_in(_tk, 500 + 1), (1000, 128), jnp.float32)
        tbl_2 = 0.05 * jax.random.normal(jax.random.fold_in(_tk, 500 + 2), (1250, 128), jnp.float32)
        tbl_3 = 0.05 * jax.random.normal(jax.random.fold_in(_tk, 500 + 3), (125000, 128), jnp.float32)
        tbl_4 = 0.05 * jax.random.normal(jax.random.fold_in(_tk, 500 + 4), (12500, 128), jnp.float32)
        tbl_5 = 0.05 * jax.random.normal(jax.random.fold_in(_tk, 500 + 5), (12500, 128), jnp.float32)
        tbl_6 = 0.05 * jax.random.normal(jax.random.fold_in(_tk, 500 + 6), (12500, 128), jnp.float32)
        tbl_7 = 0.05 * jax.random.normal(jax.random.fold_in(_tk, 500 + 7), (1250, 128), jnp.float32)
        tbl_8 = 0.05 * jax.random.normal(jax.random.fold_in(_tk, 500 + 8), (1000, 128), jnp.float32)
        tbl_9 = 0.05 * jax.random.normal(jax.random.fold_in(_tk, 500 + 9), (1000, 128), jnp.float32)
        tbl_10 = 0.05 * jax.random.normal(jax.random.fold_in(_tk, 500 + 10), (1000, 128), jnp.float32)
        tbl_11 = 0.05 * jax.random.normal(jax.random.fold_in(_tk, 500 + 11), (1250, 128), jnp.float32)
        tbl_12 = 0.05 * jax.random.normal(jax.random.fold_in(_tk, 500 + 12), (12500, 128), jnp.float32)
        tbl_13 = 0.05 * jax.random.normal(jax.random.fold_in(_tk, 500 + 13), (12500, 128), jnp.float32)
        tbl_14 = 0.05 * jax.random.normal(jax.random.fold_in(_tk, 500 + 14), (12500, 128), jnp.float32)
        tbl_15 = 0.05 * jax.random.normal(jax.random.fold_in(_tk, 500 + 15), (12500, 128), jnp.float32)
        tbl_16 = 0.05 * jax.random.normal(jax.random.fold_in(_tk, 500 + 16), (1250, 128), jnp.float32)
        tbl_17 = 0.05 * jax.random.normal(jax.random.fold_in(_tk, 500 + 17), (12500, 128), jnp.float32)
        tbl_18 = 0.05 * jax.random.normal(jax.random.fold_in(_tk, 500 + 18), (1000, 128), jnp.float32)
        tbl_19 = 0.05 * jax.random.normal(jax.random.fold_in(_tk, 500 + 19), (1000, 128), jnp.float32)
        tbl_20 = 0.05 * jax.random.normal(jax.random.fold_in(_tk, 500 + 20), (1000, 128), jnp.float32)
        tbl_21 = 0.05 * jax.random.normal(jax.random.fold_in(_tk, 500 + 21), (1250, 128), jnp.float32)
        tbl_22 = 0.05 * jax.random.normal(jax.random.fold_in(_tk, 500 + 22), (1000, 128), jnp.float32)
        tbl_23 = 0.05 * jax.random.normal(jax.random.fold_in(_tk, 500 + 23), (1250, 128), jnp.float32)
        tbl_24 = 0.05 * jax.random.normal(jax.random.fold_in(_tk, 500 + 24), (1250, 128), jnp.float32)
        tbl_25 = 0.05 * jax.random.normal(jax.random.fold_in(_tk, 500 + 25), (1000, 128), jnp.float32)
        _rk = jax.random.fold_in(_tk, 7)
        r_dense_x = -0.000514642 + 1.00011 * jax.random.normal(jax.random.fold_in(_rk, 101), (512, 128), jnp.float32)
        W_top1 = 0.0456912 * jax.random.normal(jax.random.fold_in(_tk, 801), (479, 512), jnp.float32)
        W_top2 = 0.0441942 * jax.random.normal(jax.random.fold_in(_tk, 802), (512, 256), jnp.float32)
        W_top3 = 0.0625 * jax.random.normal(jax.random.fold_in(_tk, 803), (256, 1), jnp.float32)
        b_top1 = jnp.zeros((512,), jnp.float32)
        b_top2 = jnp.zeros((256,), jnp.float32)
        return (r_dense_x, ids, tbl_0, tbl_1, tbl_2, tbl_3, tbl_4, tbl_5, tbl_6, tbl_7, tbl_8, tbl_9, tbl_10, tbl_11, tbl_12, tbl_13, tbl_14, tbl_15, tbl_16, tbl_17, tbl_18, tbl_19, tbl_20, tbl_21, tbl_22, tbl_23, tbl_24, tbl_25, W_top1, b_top1, W_top2, b_top2, W_top3)
    r_dense_x, ids, tbl_0, tbl_1, tbl_2, tbl_3, tbl_4, tbl_5, tbl_6, tbl_7, tbl_8, tbl_9, tbl_10, tbl_11, tbl_12, tbl_13, tbl_14, tbl_15, tbl_16, tbl_17, tbl_18, tbl_19, tbl_20, tbl_21, tbl_22, tbl_23, tbl_24, tbl_25, W_top1, b_top1, W_top2, b_top2, W_top3 = _rec_inputs()

    def _L0_rec_setup():
        import jax, jax.numpy as jnp
        import numpy as np
        F = 26
        D = 128
        B = 2048
        _TRIU_I, _TRIU_J = np.triu_indices(F + 1, k=1)
        _TRIU_I = jnp.asarray(_TRIU_I)
        _TRIU_J = jnp.asarray(_TRIU_J)
        key = jax.random.key(seed)
        k1, k2 = jax.random.split(key)
        sparse_x = jax.random.normal(k1, (B, F, D), dtype=jnp.float32)
        dense_x = jax.random.normal(k2, (B, D), dtype=jnp.float32)
        return {'sparse_x': sparse_x, 'dense_x': dense_x}
    _L0_rec_all = _L0_rec_setup()
    _L0_rec_in = {k: v for k, v in _L0_rec_all.items() if k in ()}
    del _L0_rec_all
    return {'r_dense_x': r_dense_x, 'ids': ids, 'tbl_0': tbl_0, 'tbl_1': tbl_1, 'tbl_2': tbl_2, 'tbl_3': tbl_3, 'tbl_4': tbl_4, 'tbl_5': tbl_5, 'tbl_6': tbl_6, 'tbl_7': tbl_7, 'tbl_8': tbl_8, 'tbl_9': tbl_9, 'tbl_10': tbl_10, 'tbl_11': tbl_11, 'tbl_12': tbl_12, 'tbl_13': tbl_13, 'tbl_14': tbl_14, 'tbl_15': tbl_15, 'tbl_16': tbl_16, 'tbl_17': tbl_17, 'tbl_18': tbl_18, 'tbl_19': tbl_19, 'tbl_20': tbl_20, 'tbl_21': tbl_21, 'tbl_22': tbl_22, 'tbl_23': tbl_23, 'tbl_24': tbl_24, 'tbl_25': tbl_25, 'W_top1': W_top1, 'b_top1': b_top1, 'W_top2': W_top2, 'b_top2': b_top2, 'W_top3': W_top3}

def reference(r_dense_x, ids, tbl_0, tbl_1, tbl_2, tbl_3, tbl_4, tbl_5, tbl_6, tbl_7, tbl_8, tbl_9, tbl_10, tbl_11, tbl_12, tbl_13, tbl_14, tbl_15, tbl_16, tbl_17, tbl_18, tbl_19, tbl_20, tbl_21, tbl_22, tbl_23, tbl_24, tbl_25, W_top1, b_top1, W_top2, b_top2, W_top3):
    import jax
    import jax.numpy as jnp

    def _L0_rec_ref(sparse_x, dense_x):
        import jax, jax.numpy as jnp
        import numpy as np
        F = 26
        D = 128
        B = 2048
        _TRIU_I, _TRIU_J = np.triu_indices(F + 1, k=1)
        _TRIU_I = jnp.asarray(_TRIU_I)
        _TRIU_J = jnp.asarray(_TRIU_J)
        combined = jnp.concatenate([sparse_x, dense_x[:, None, :]], axis=1)
        interact = jnp.einsum('bfd,bgd->bfg', combined, combined)
        return interact[:, _TRIU_I, _TRIU_J]
    e = jnp.stack([tbl_0[ids[:, 0]], tbl_1[ids[:, 1]], tbl_2[ids[:, 2]], tbl_3[ids[:, 3]], tbl_4[ids[:, 4]], tbl_5[ids[:, 5]], tbl_6[ids[:, 6]], tbl_7[ids[:, 7]], tbl_8[ids[:, 8]], tbl_9[ids[:, 9]], tbl_10[ids[:, 10]], tbl_11[ids[:, 11]], tbl_12[ids[:, 12]], tbl_13[ids[:, 13]], tbl_14[ids[:, 14]], tbl_15[ids[:, 15]], tbl_16[ids[:, 16]], tbl_17[ids[:, 17]], tbl_18[ids[:, 18]], tbl_19[ids[:, 19]], tbl_20[ids[:, 20]], tbl_21[ids[:, 21]], tbl_22[ids[:, 22]], tbl_23[ids[:, 23]], tbl_24[ids[:, 24]], tbl_25[ids[:, 25]]], axis=1)
    z = _L0_rec_ref(e, r_dense_x)
    z = z.reshape(z.shape[0], -1)
    h = jnp.concatenate([z, r_dense_x], axis=1)
    h = jnp.maximum(h @ W_top1 + b_top1, 0.0)
    h = jnp.maximum(h @ W_top2 + b_top2, 0.0)
    y = h @ W_top3
    return y

_drawn_inputs = setup_inputs


def setup_inputs(seed=0):
    import zlib

    import numpy as np

    out = dict(_drawn_inputs(seed))
    spreads = {'b_top1': (0.0, 0.1), 'b_top2': (0.0, 0.1)}
    factors = {}
    for name, (base, spread) in spreads.items():
        noise = np.random.default_rng([zlib.crc32(name.encode()), seed]).standard_normal(out[name].shape)
        drawn = base * np.exp(spread * noise) if base else spread * noise
        out[name] = jnp.asarray(drawn.astype(out[name].dtype))
    for name, factor in factors.items():
        out[name] = (out[name] * factor).astype(out[name].dtype)
    return out
```

```python
from contextlib import ExitStack

import concourse.bass as bass
from concourse import mybir

F32 = mybir.dt.float32
I32 = mybir.dt.int32
ALU = mybir.AluOpType
ACT = mybir.ActivationFunctionType

P = 128
BATCH = 512
TILES = BATCH // P
FEATURES = 26
DIM = 128
SLOTS = FEATURES + 1
N1, N2 = 512, 256
C1, C2 = N1 // P, N2 // P

ONEHOT = [1, 8, 9, 10]
ROWS = 1000
RP = 125
RC = ROWS // RP
GATHERED = [f for f in range(FEATURES) if f not in ONEHOT]
SLOT_OF = ONEHOT + GATHERED + [FEATURES]

GROUP = 4
GROUPS = -(-SLOTS // GROUP)
HALF = 3
S = 4
R = P // S
FP = 32
QUADS = 4
RQ = R // QUADS
J = 4
NI = -(-SLOTS // J)
RECT = [2 * i * (i - 1) for i in range(NI + 1)]
PLACES = RECT[NI] + (J - 1) * NI
BANK = 512


def pair_places():
    for g in range(SLOTS):
        i, j = divmod(g, J)
        for f in range(g):
            place = RECT[i] + f if f < J * i else RECT[NI] + (J - 1) * i + f - J * i
            yield place, j, f, g


def dlrm_tower(nc, dense, ids, tables, w1_pairs, w1_dense, b1, w2, b2, w3, out):
    with ExitStack() as ctx:
        def sb(name, shape, dt=F32):
            return ctx.enter_context(nc.sbuf_tensor(name, shape, dt))

        def sem(name):
            return ctx.enter_context(nc.semaphore(name))

        ones = sb("ones", [P, P])
        ident = sb("ident", [P, P])
        row_id = sb("row_id", [P, RC])
        table_sb = [sb(f"table{k}", [RP, RC * DIM]) for k in range(len(ONEHOT))]
        w1p_sb = sb("w1p_sb", [PLACES, J, N1])
        w1d_sb = sb("w1d_sb", [DIM, N1])
        w2_sb = sb("w2_sb", [P, C1, N2])
        w3_sb = sb("w3_sb", [P, C2])
        b1_sb = sb("b1_sb", [P, C1])
        b2_sb = sb("b2_sb", [P, C2])
        idx = [sb(f"idx{h}", [P, FEATURES], I32) for h in range(2)]
        ids_all = sb("ids_all", [P, TILES, FEATURES], I32)
        ids_f = sb("ids_f", [P, TILES, len(ONEHOT)])
        diag = sb("diag", [P, len(ONEHOT), P])
        onehot = sb("onehot", [RP, len(ONEHOT), RC, P])
        x = sb("x", [P, SLOTS, DIM])
        xt = sb("xt", [P, P, FP])
        dense_t = sb("dense_t", [P, S, R])
        gram = sb("gram", [P, SLOTS, R])
        pairs = sb("pairs", [P, S, PLACES])
        zt = sb("zt", [PLACES, S, J, R])
        h1 = sb("h1", [P, C1, P])
        h2 = sb("h2", [P, C2, P])
        y_row = sb("y_row", [1, BATCH])

        bank_t = [ctx.enter_context(nc.psum_tensor(f"bank_t{i}", [P, BANK], F32)) for i in range(2)]
        bank_g = [ctx.enter_context(nc.psum_tensor(f"bank_g{i}", [P, 2, BANK], F32)) for i in range(2)]
        bank_m = [ctx.enter_context(nc.psum_tensor(f"bank_m{i}", [P, BANK], F32)) for i in range(2)]

        idx_loaded = [sem(f"idx_loaded{h}") for h in range(2)]
        dense_loaded = sem("dense_loaded")
        ids_loaded = sem("ids_loaded")
        tables_loaded = sem("tables_loaded")
        weights_loaded = sem("weights_loaded")
        landed = {s: sem(f"landed{s}") for s in range(len(ONEHOT), FEATURES)}
        ones_ready = sem("ones_ready")
        const_ready = sem("const_ready")
        pads_ready = sem("pads_ready")
        ids_f_ready = sem("ids_f_ready")
        diag_ready = sem("diag_ready")
        id_rows_ready = sem("id_rows_ready")
        onehot_ready = sem("onehot_ready")
        group_ready = sem("group_ready")
        xt_dve, xt_act = sem("xt_dve"), sem("xt_act")
        gram_ready = sem("gram_ready")
        gram_dve, gram_act = sem("gram_dve"), sem("gram_act")
        fold_ready = sem("fold_ready")
        pairs_dve, pairs_act = sem("pairs_dve"), sem("pairs_act")
        zt_ready = sem("zt_ready")
        zt_dve, zt_act = sem("zt_dve"), sem("zt_act")
        h1_ready = sem("h1_ready")
        h1_dve, h1_act = sem("h1_dve"), sem("h1_act")
        h2_ready = sem("h2_ready")
        h2_dve, h2_act = sem("h2_dve"), sem("h2_act")
        y_ready = sem("y_ready")
        y_done = sem("y_done")
        stored = sem("stored")

        ids_tiles = ids.rearrange("(p t) f -> p t f", t=TILES)
        dense_tiles = dense.rearrange("(p t) d -> p t d", t=TILES)
        XT_DVE = GROUPS // 2 + 2
        XT_ACT = GROUPS // 2

        def group_slots(g):
            return range(GROUP * g, min(GROUP * g + GROUP, SLOTS))

        block = ctx.enter_context(nc.Block())

        @block.sync
        def _(sp):
            sp.dma_start(idx[0][:, :], ids_tiles[:, 0, :]).then_inc(idx_loaded[0], 16)
            sp.dma_start(idx[1][:, :], ids_tiles[:, 0, :]).then_inc(idx_loaded[1], 16)
            sp.dma_start(ids_all[:, :, :], ids_tiles).then_inc(ids_loaded, 16)
            sp.dma_start(x[:, FEATURES, :], dense_tiles[:, 0, :]).then_inc(dense_loaded, 16)
            for k, f in enumerate(ONEHOT):
                sp.dma_start(table_sb[k][:, :], tables[f].rearrange("(p c) d -> p (c d)", c=RC)).then_inc(tables_loaded, 16)
            with sp.Fori(1, TILES) as t:
                sp.wait_ge(group_ready, GROUPS * t - (GROUPS - 1 - HALF))
                sp.nop(nofuse=True)
                sp.dma_start(idx[0][:, :], ids_tiles[:, bass.ds(t, 1), :]).then_inc(idx_loaded[0], 16)
                sp.wait_ge(group_ready, GROUPS * t)
                sp.nop(nofuse=True)
                sp.dma_start(idx[1][:, :], ids_tiles[:, bass.ds(t, 1), :]).then_inc(idx_loaded[1], 16)
                sp.dma_start(x[:, FEATURES, :], dense_tiles[:, bass.ds(t, 1), :]).then_inc(dense_loaded, 16)
            sp.wait_ge(y_done, TILES)
            sp.dma_start(out.rearrange("b o -> o b"), y_row[:, :]).then_inc(stored, 16)
            sp.wait_ge(stored, 16)

        @block.gpsimd
        def _(pool):
            pool.wait_ge(ones_ready, 1)
            pool.affine_select(out=ident[:, :], in_=ones[:, :], compare_op=ALU.is_equal, fill=0.0, base=0,
                               pattern=[[-1, P]], channel_multiplier=1).then_inc(const_ready, 1)
            pool.iota(row_id[:, :], [[1, RC]], base=0, channel_multiplier=RC,
                      allow_small_or_imprecise_dtypes=True).then_inc(const_ready, 1)
            with pool.Fori(0, TILES) as t:
                for h in range(2):
                    pool.wait_ge(idx_loaded[h], 16 * t + 16)
                    pool.nop(nofuse=True)
                    for g in (range(1, HALF + 1) if h == 0 else range(HALF + 1, GROUPS)):
                        for s in group_slots(g):
                            if s < FEATURES:
                                f = SLOT_OF[s]
                                pool.indirect_dma_start(
                                    x[:, s, :], None, tables[f][:, :],
                                    bass.IndirectOffsetOnAxis(ap=idx[h][:, f:f + 1], axis=0)).then_inc(landed[s], 16)

        @block.tensor
        def _(pe):
            def id_rows(t):
                pe.wait_ge(diag_ready, t + 1)
                pe.matmul(bank_t[1][:, :], ones[:, :], diag[:, :, :], start=True, stop=True).then_inc(id_rows_ready, 1)

            def look_up(t):
                for k in range(len(ONEHOT)):
                    pe.wait_ge(onehot_ready, len(ONEHOT) * t + k + 1)
                    for c in range(RC):
                        mm = pe.matmul(bank_t[0][:, k * P:(k + 1) * P], table_sb[k][:, c * DIM:(c + 1) * DIM],
                                       onehot[:, k, c, :], start=(c == 0), stop=(c == RC - 1))
                mm.then_inc(group_ready, 1)

            def turn_group(t, g):
                if g >= 3 and g % 2 == 1:
                    pe.wait_ge(xt_act, XT_ACT * t + g // 2)
                if g >= 2 and g % 2 == 0:
                    pe.wait_ge(xt_dve, XT_DVE * t + g // 2)
                for n, s in enumerate(group_slots(g)):
                    if s < FEATURES:
                        pe.wait_ge(landed[s], 16 * t + 16)
                    else:
                        pe.wait_ge(dense_loaded, 16 * t + 16)
                    mm = pe.transpose(bank_t[g % 2][:, n * P:(n + 1) * P], x[:, s, :], ident[:, :])
                mm.then_inc(group_ready, 1)

            def grams(t):
                pe.wait_ge(xt_dve, XT_DVE * t + XT_DVE)
                pe.wait_ge(xt_act, XT_ACT * t + XT_ACT)
                for q in range(QUADS):
                    if q >= 2:
                        pe.wait_ge(gram_dve, QUADS * t + q - 1)
                        pe.wait_ge(gram_act, QUADS * t + q - 1)
                    for n in range(RQ):
                        p0 = S * (q * RQ + n)
                        at = SLOTS * S * (n % GROUP)
                        mm = pe.matmul(bank_g[q % 2][:, n // GROUP, at:at + SLOTS * S], xt[:, p0:p0 + S, :],
                                       xt[:, p0:p0 + S, 0:SLOTS], start=True, stop=True)
                    mm.then_inc(gram_ready, 1)

            def fold(t):
                pe.wait_ge(gram_dve, QUADS * t + QUADS)
                pe.wait_ge(gram_act, QUADS * t + QUADS)
                for i in range(NI):
                    g0, g1 = J * i, min(J * i + J, SLOTS)
                    mm = pe.transpose(bank_g[0][0:(g1 - g0) * R, i // GROUP, (i % GROUP) * P:(i % GROUP + 1) * P],
                                      gram[:, g0:g1, :], ident[:, :])
                    if i % GROUP == GROUP - 1 or i == NI - 1:
                        mm.then_inc(fold_ready, 1)

            def turn_pairs(t):
                pe.wait_ge(pairs_dve, t + 1)
                pe.wait_ge(pairs_act, t + 1)
                for s in range(S):
                    mm = pe.transpose(bank_g[1][0:PLACES, s // 2, (s % 2) * P:(s % 2 + 1) * P],
                                      pairs[:, s, :], ident[:, :])
                    if s % 2 == 1:
                        mm.then_inc(zt_ready, 1)

            def layer_1(t):
                for n in range(C1):
                    pe.matmul(bank_m[n // 2][:, (n % 2) * P:(n % 2 + 1) * P], w1d_sb[:, n * P:(n + 1) * P],
                              dense_t[:, :, :], start=(n % 2 == 0), stop=False, skip_group_check=True)
                pe.wait_ge(zt_dve, t + 1)
                pe.wait_ge(zt_act, t + 1)
                for n in range(C1):
                    for j in range(J):
                        mm = pe.matmul(bank_m[n // 2][:, (n % 2) * P:(n % 2 + 1) * P], w1p_sb[:, j, n * P:(n + 1) * P],
                                       zt[:, :, j, :], start=False, stop=(j == J - 1), skip_group_check=True)
                    if n % 2 == 1:
                        mm.then_inc(h1_ready, 1)

            def layer_2(t):
                for n in range(C1):
                    if n == 0:
                        pe.wait_ge(h1_dve, t + 1)
                    if n == 2:
                        pe.wait_ge(h1_act, t + 1)
                    for m in range(C2):
                        mm = pe.matmul(bank_g[0][:, m, 0:P], w2_sb[:, n, m * P:(m + 1) * P], h1[:, n, :],
                                       start=(n == 0), stop=(n == C1 - 1))
                        if n == C1 - 1:
                            mm.then_inc(h2_ready, 1)

            def layer_3(t):
                pe.wait_ge(h2_dve, t + 1)
                pe.wait_ge(h2_act, t + 1)
                for m in range(C2):
                    mm = pe.matmul(bank_m[0][0:1, 0:P], w3_sb[:, m:m + 1], h2[:, m, :], start=(m == 0), stop=(m == C2 - 1))
                mm.then_inc(y_ready, 1)

            pe.wait_ge(const_ready, 2)
            pe.wait_ge(pads_ready, 2)
            pe.wait_ge(tables_loaded, 16 * len(ONEHOT))
            pe.wait_ge(weights_loaded, 16 * 6)
            with pe.Fori(0, TILES) as t:
                id_rows(t)
                look_up(t)
                for g in range(1, GROUPS):
                    turn_group(t, g)
                grams(t)
                fold(t)
                turn_pairs(t)
                layer_1(t)
                layer_2(t)
                layer_3(t)

        def move_group(eng_copy, g):
            slots = group_slots(g)
            n = len(slots)
            return eng_copy(xt[:, :, slots[0]:slots[0] + n],
                            bank_t[g % 2][:, 0:n * P].rearrange("d (s p) -> d p s", p=P))

        def move_gram(eng_copy, q, s):
            rows = slice(FP * s, FP * s + FP)
            src = bank_g[q % 2][rows, :, 0:GROUP * S * SLOTS].rearrange("f b (r s g) -> f b r s g", r=GROUP, s=S)
            dst = gram[rows, :, q * RQ:(q + 1) * RQ].rearrange("f g (b r) -> f b r g", b=2)
            return eng_copy(dst, src[:, :, :, s, :])

        def move_pairs(eng_copy, b):
            i0, i1 = GROUP * b, min(GROUP * b + GROUP, NI)
            for i in range(max(i0, 1), i1):
                np_ = (min(J * i + J, SLOTS) - J * i) * R
                src = bank_g[0][0:np_, b, (i - i0) * P:(i - i0 + 1) * P].rearrange("p (s f) -> p s f", s=S)
                eng_copy(pairs[0:np_, :, RECT[i]:RECT[i + 1]], src[:, :, 0:J * i])
            for j in range(1, J):
                n = (i1 if J * (i1 - 1) + j < SLOTS else i1 - 1) - i0
                rows = slice(R * j, R * j + R)
                src = bank_g[0][rows, b, 0:BANK].rearrange("p (i s f) -> p i s f", i=GROUP, s=S)
                dst = pairs[rows, :, RECT[NI]:].rearrange("p s (i f) -> p i s f", f=J - 1)
                for f in range(j):
                    start = J * i0 + f
                    last = eng_copy(dst[:, i0:i0 + n, :, f],
                                    diagonal(bank_g[0], rows, b, start, n))
            return last

        def diagonal(bank, rows, b, start, n):
            flat = bank[rows, b, :]
            ap = bass.AP(flat.tensor, flat.offset + start, [list(flat.ap[0]), [P + J, n], [FP, S]])
            return ap

        @block.vector
        def _(dve):
            def copy(o, i):
                return dve.tensor_copy(o, i)

            def make_onehots(t):
                dve.tensor_tensor(diag[:, :, :], ident[:, None, :].to_broadcast([P, len(ONEHOT), P]),
                                  ids_f[:, bass.ds(t, 1), :].rearrange("p a k -> p (a k)")[:, :, None].to_broadcast([P, len(ONEHOT), P]),
                                  ALU.mult).then_inc(diag_ready, 1)
                dve.wait_ge(id_rows_ready, t + 1)
                for k in range(len(ONEHOT)):
                    dve.tensor_tensor(onehot[:, k, :, :],
                                      bank_t[1][0:RP, None, k * P:(k + 1) * P].to_broadcast([RP, RC, P]),
                                      row_id[0:RP, :, None].to_broadcast([RP, RC, P]),
                                      ALU.is_equal).then_inc(onehot_ready, 1)

            dve.memset(ones[:, :], 1.0).then_inc(ones_ready, 1)
            dve.memset(xt[:, :, SLOTS:], 0.0).then_inc(pads_ready, 1)
            dve.memset(pairs[:, :, :], 0.0).then_inc(pads_ready, 1)
            dve.wait_ge(ids_loaded, 16)
            for k, f in enumerate(ONEHOT):
                dve.tensor_copy(ids_f[:, :, k:k + 1], ids_all[:, :, f:f + 1]).then_inc(ids_f_ready, 1)
            dve.wait_ge(ids_f_ready, len(ONEHOT))
            dve.wait_ge(const_ready, 2)
            dve.wait_ge(pads_ready, 2)
            dve.wait_ge(weights_loaded, 16 * 6)
            with dve.Fori(0, TILES) as t:
                make_onehots(t)
                for g in range(0, GROUPS, 2):
                    dve.wait_ge(group_ready, GROUPS * t + g + 1)
                    move_group(copy, g).then_inc(xt_dve, 1)
                n = FEATURES % GROUP
                dve.tensor_copy(dense_t[:, :, :], bank_t[0][:, n * P:(n + 1) * P].rearrange("d (r s) -> d s r", s=S)).then_inc(xt_dve, 1)
                for q in range(QUADS):
                    dve.wait_ge(gram_ready, QUADS * t + q + 1)
                    move_gram(copy, q, 0)
                    move_gram(copy, q, 1).then_inc(gram_dve, 1)
                dve.wait_ge(fold_ready, 2 * t + 1)
                move_pairs(copy, 0).then_inc(pairs_dve, 1)
                dve.wait_ge(zt_ready, 2 * t + 1)
                dve.tensor_copy(zt[:, 0:2, :, :], bank_g[1][0:PLACES, 0, 0:2 * P]).then_inc(zt_dve, 1)
                dve.wait_ge(h1_ready, 2 * t + 1)
                for n in range(2):
                    last = dve.tensor_scalar(h1[:, n, :], bank_m[0][:, n * P:(n + 1) * P], b1_sb[:, n:n + 1], 0.0,
                                             ALU.add, ALU.max)
                last.then_inc(h1_dve, 1)
                dve.wait_ge(h2_ready, 2 * t + 1)
                dve.tensor_scalar(h2[:, 0, :], bank_g[0][:, 0, 0:P], b2_sb[:, 0:1], 0.0, ALU.add, ALU.max).then_inc(h2_dve, 1)
                dve.wait_ge(y_ready, t + 1)
                dve.tensor_copy(y_row.rearrange("o (r s t) -> o t s r", s=S, t=TILES)[:, bass.ds(t, 1), :, :],
                                bank_m[0][0:1, 0:P].rearrange("o (s r) -> o s r", s=S)).then_inc(y_done, 1)

        @block.scalar
        def _(act):
            def copy(o, i):
                return act.copy(o, i)

            act.dma_start(w1p_sb[:, :, :], w1_pairs).then_inc(weights_loaded, 16)
            act.dma_start(w1d_sb[:, :], w1_dense).then_inc(weights_loaded, 16)
            act.dma_start(w2_sb[:, :, :], w2.rearrange("(c p) n -> p c n", p=P)).then_inc(weights_loaded, 16)
            act.dma_start(w3_sb[:, :], w3).then_inc(weights_loaded, 16)
            act.dma_start(b1_sb[:, :], b1).then_inc(weights_loaded, 16)
            act.dma_start(b2_sb[:, :], b2).then_inc(weights_loaded, 16)
            act.wait_ge(weights_loaded, 16 * 6)
            act.wait_ge(pads_ready, 2)
            with act.Fori(0, TILES) as t:
                for g in range(1, GROUPS, 2):
                    act.wait_ge(group_ready, GROUPS * t + g + 1)
                    move_group(copy, g).then_inc(xt_act, 1)
                for q in range(QUADS):
                    act.wait_ge(gram_ready, QUADS * t + q + 1)
                    move_gram(copy, q, 2)
                    move_gram(copy, q, 3).then_inc(gram_act, 1)
                act.wait_ge(fold_ready, 2 * t + 2)
                move_pairs(copy, 1).then_inc(pairs_act, 1)
                act.wait_ge(zt_ready, 2 * t + 2)
                act.copy(zt[:, 2:4, :, :], bank_g[1][0:PLACES, 1, 0:2 * P]).then_inc(zt_act, 1)
                act.wait_ge(h1_ready, 2 * t + 2)
                for n in range(2, 4):
                    last = act.activation(h1[:, n, :], bank_m[1][:, (n - 2) * P:(n - 1) * P], ACT.Relu, bias=b1_sb[:, n:n + 1])
                last.then_inc(h1_act, 1)
                act.wait_ge(h2_ready, 2 * t + 2)
                act.activation(h2[:, 1, :], bank_g[0][:, 1, 0:P], ACT.Relu, bias=b2_sb[:, 1:2]).then_inc(h2_act, 1)


def kernel(**inputs):
    import numpy as np
    import concourse.bacc as bacc
    from concourse.bass_utils import run_bass_kernel_spmd

    w1 = np.asarray(inputs["W_top1"])
    n_pairs = SLOTS * (SLOTS - 1) // 2
    w1_pairs = np.zeros((PLACES, J, N1), w1.dtype)
    for place, j, f, g in pair_places():
        a, b = sorted((SLOT_OF[f], SLOT_OF[g]))
        w1_pairs[place, j] = w1[a * SLOTS - a * (a + 1) // 2 + b - a - 1]
    data = {
        "dense": np.asarray(inputs["r_dense_x"]),
        "ids": np.asarray(inputs["ids"]),
        "w1_pairs": w1_pairs,
        "w1_dense": w1[n_pairs:],
        "b1": np.asarray(inputs["b_top1"]).reshape(C1, P).T,
        "w2": np.asarray(inputs["W_top2"]),
        "b2": np.asarray(inputs["b_top2"]).reshape(C2, P).T,
        "w3": np.asarray(inputs["W_top3"]).reshape(C2, P).T,
    }
    for f in range(FEATURES):
        data[f"table_{f}"] = np.asarray(inputs[f"tbl_{f}"])

    nc = bacc.Bacc("TRN2", target_bir_lowering=False, num_devices=1)
    arrays, aps = {}, {}
    for name, a in data.items():
        arrays[f"in_{name}"] = np.ascontiguousarray(a)
        aps[name] = nc.dram_tensor(f"in_{name}", a.shape, mybir.dt.from_np(a.dtype), kind="ExternalInput").ap()
    out = nc.dram_tensor("out_y", (BATCH, 1), F32, kind="ExternalOutput").ap()
    dlrm_tower(nc, aps["dense"], aps["ids"], [aps[f"table_{f}"] for f in range(FEATURES)], aps["w1_pairs"],
               aps["w1_dense"], aps["b1"], aps["w2"], aps["b2"], aps["w3"], out)
    r = run_bass_kernel_spmd(nc, [arrays], core_ids=[0])
    return r.results[0]["out_y"]
```

```python
from contextlib import ExitStack

import concourse.bass as bass
from concourse import mybir

F32 = mybir.dt.float32
I32 = mybir.dt.int32
U32 = mybir.dt.uint32
F32R = mybir.dt.float32r
HIGH_BITS = 0xFFFFF000
ALU = mybir.AluOpType
ACT = mybir.ActivationFunctionType

P = 128
BATCH = 512
TILES = BATCH // P
FEATURES = 26
DIM = 128
SLOTS = FEATURES + 1
N1, N2 = 512, 256
C1, C2 = N1 // P, N2 // P

ONEHOT = [1, 8, 9, 10, 18]
ROWS = 1000
RP = 125
RC = ROWS // RP
K = len(ONEHOT)
GATHERED = [f for f in range(FEATURES) if f not in ONEHOT]
SLOT_OF = ONEHOT + GATHERED + [FEATURES]

GROUP = 4
GROUPS = -(-(SLOTS - K) // GROUP)
PAIR = 2
BATCHES = -(-K // 2)
WHOLE = 2
SPLIT = [*range(WHOLE, K), *range(WHOLE)]
S = 4
R = P // S
FP = 32
QUADS = 4
RQ = R // QUADS
J = 4
NI = -(-SLOTS // J)
RECT = [2 * i * (i - 1) for i in range(NI + 1)]
PLACES = RECT[NI] + (J - 1) * NI
BANK = 512


def pair_places():
    for g in range(SLOTS):
        i, j = divmod(g, J)
        for f in range(g):
            place = RECT[i] + f if f < J * i else RECT[NI] + (J - 1) * i + f - J * i
            yield place, j, f, g


def dlrm_tower(nc, dense, ids, tables, w1_pairs, w1_dense, b1, w2, b2, w3, out):
    with ExitStack() as ctx:
        def sb(name, shape, dt=F32):
            return ctx.enter_context(nc.sbuf_tensor(name, shape, dt))

        def sem(name):
            return ctx.enter_context(nc.semaphore(name))

        ones = sb("ones", [P, P])
        ones_r = sb("ones_r", [P, P], F32R)
        ident = sb("ident", [P, P])
        row_id = sb("row_id", [P, RC])
        raw = [sb(f"raw{k}", [RP, RC * DIM]) for k in range(K)]
        upper = [sb(f"upper{i}", [RP, RC * DIM]) for i in range(2)]
        table_hi = [sb(f"table_hi{k}", [RP, RC * DIM], F32R) for k in range(K)]
        table_lo = [sb(f"table_lo{k}", [RP, RC * DIM], F32R) for k in range(K)]
        w1p_sb = sb("w1p_sb", [PLACES, J, N1])
        w1d_sb = sb("w1d_sb", [DIM, N1])
        w2_sb = sb("w2_sb", [P, C1, N2])
        w3_sb = sb("w3_sb", [P, C2])
        b1_sb = sb("b1_sb", [P, C1])
        b2_sb = sb("b2_sb", [P, C2])
        ids_sb = sb("ids_sb", [P, TILES, FEATURES], I32)
        ids_f = sb("ids_f", [P, TILES, K])
        diag = [sb(f"diag{b}", [P, 2, PAIR, P], F32R) for b in range(2)]
        onehot = [sb(f"onehot{b}", [RP, 2, RC, PAIR * P], F32R) for b in range(2)]
        dense_sb = sb("dense_sb", [P, TILES, DIM])
        x = [sb(f"x{b}", [P, FEATURES - K, DIM]) for b in range(2)]
        xt = [sb(f"xt{b}", [P, P, FP]) for b in range(2)]
        dense_t = sb("dense_t", [P, S, R])
        gram = sb("gram", [P, SLOTS, R])
        pairs = sb("pairs", [P, S, PLACES])
        zt = sb("zt", [PLACES, S, J, R])
        h1 = sb("h1", [P, C1, P])
        h2 = sb("h2", [P, C2, P])
        y_row = sb("y_row", [1, BATCH])

        bank_t = [ctx.enter_context(nc.psum_tensor(f"bank_t{i}", [P, BANK], F32)) for i in range(2)]
        bank_g = [ctx.enter_context(nc.psum_tensor(f"bank_g{i}", [P, 2, BANK], F32)) for i in range(2)]
        bank_m = [ctx.enter_context(nc.psum_tensor(f"bank_m{i}", [P, BANK], F32)) for i in range(2)]

        dense_loaded = sem("dense_loaded")
        ids_loaded = sem("ids_loaded")
        table_loaded = [sem(f"table_loaded{k}") for k in range(K)]
        upper_ready = sem("upper_ready")
        hi_ready = sem("hi_ready")
        lo_ready = sem("lo_ready")
        weights_loaded = sem("weights_loaded")
        landed = [{s: sem(f"landed{b}_{s}") for s in range(K, FEATURES)} for b in range(2)]
        ones_ready = sem("ones_ready")
        const_ready = sem("const_ready")
        pads_ready = sem("pads_ready")
        ids_f_ready = sem("ids_f_ready")
        diag_ready = sem("diag_ready")
        id_rows_ready = sem("id_rows_ready")
        onehot_ready = sem("onehot_ready")
        looked_up = sem("looked_up")
        embedded = sem("embedded")
        group_ready = sem("group_ready")
        dense_moved = sem("dense_moved")
        xt_dve, xt_act = sem("xt_dve"), sem("xt_act")
        gram_ready = sem("gram_ready")
        gram_dve, gram_act = sem("gram_dve"), sem("gram_act")
        fold_ready = sem("fold_ready")
        pairs_dve, pairs_act = sem("pairs_dve"), sem("pairs_act")
        zt_ready = sem("zt_ready")
        zt_dve, zt_act = sem("zt_dve"), sem("zt_act")
        h1_ready = sem("h1_ready")
        h1_dve, h1_act = sem("h1_dve"), sem("h1_act")
        h2_ready = sem("h2_ready")
        h2_dve, h2_act = sem("h2_dve"), sem("h2_act")
        y_ready = sem("y_ready")
        y_done = sem("y_done")
        stored = sem("stored")

        ids_tiles = ids.rearrange("(p t) f -> p t f", t=TILES)
        dense_tiles = dense.rearrange("(p t) d -> p t d", t=TILES)

        def group_slots(g):
            return range(K + GROUP * g, min(K + GROUP * g + GROUP, SLOTS))

        def early_groups(t):
            return (0, 4, 2, 4)[t]

        def group_bank(t, g):
            if g < early_groups(t):
                return bank_t[g % 2][:, :]
            return (bank_g[0][:, 0, :], bank_g[0][:, 1, :], bank_g[1][:, 0, :], bank_g[1][:, 1, :],
                    bank_m[0][:, :], bank_m[1][:, :])[g]

        def id_row_bank(u, b):
            return bank_m[0] if (u, b) == (0, 2) else bank_t[batch_of[u, b] % 2]

        def dve_groups(t):
            return range(0, (0, 4, GROUPS, GROUPS)[t], 2)

        def groups_moved(t):
            by_dve = sum(len(dve_groups(i)) for i in range(t + 1))
            return by_dve, GROUPS * (t + 1) - by_dve

        def batch_tables(b):
            return range(2 * b, min(2 * b + 2, K))

        split_place = {k: n for n, k in enumerate(SPLIT)}

        batches = [(u, b) for u in range(TILES // PAIR) for b in range(BATCHES)]
        batch_of = {ub: n for n, ub in enumerate(batches)}

        block = ctx.enter_context(nc.Block())

        @block.sync
        def _(sp):
            sp.dma_start(ids_sb[:, :, :], ids_tiles).then_inc(ids_loaded, 16)
            for k, f in enumerate(ONEHOT):
                sp.dma_start(raw[k][:, :], tables[f].rearrange("(p c) d -> p (c d)", c=RC)).then_inc(table_loaded[k], 16)
            sp.wait_ge(y_done, TILES)
            sp.dma_start(out.rearrange("b o -> o b"), y_row[:, :]).then_inc(stored, 16)
            sp.wait_ge(stored, 16)

        @block.gpsimd
        def _(pool):
            pool.wait_ge(ones_ready, 1)
            pool.affine_select(out=ident[:, :], in_=ones[:, :], compare_op=ALU.is_equal, fill=0.0, base=0,
                               pattern=[[-1, P]], channel_multiplier=1).then_inc(const_ready, 1)
            pool.iota(row_id[:, :], [[1, RC]], base=0, channel_multiplier=RC,
                      allow_small_or_imprecise_dtypes=True).then_inc(const_ready, 1)
            pool.wait_ge(ids_loaded, 16)
            for t in range(TILES):
                for g in range(GROUPS):
                    if t >= 2:
                        pool.wait_ge(group_ready, GROUPS * (t - 2) + g + 1)
                    for s in group_slots(g):
                        if s < FEATURES:
                            f = SLOT_OF[s]
                            pool.indirect_dma_start(
                                x[t % 2][:, s - K, :], None, tables[f][:, :],
                                bass.IndirectOffsetOnAxis(ap=ids_sb[:, t, f:f + 1], axis=0)).then_inc(landed[t % 2][s], 16)

        @block.tensor
        def _(pe):
            def id_rows(u, b):
                n = batch_of[u, b]
                pe.wait_ge(diag_ready, n + 1)
                if (u, b) == (1, 0) or (u, b) == (1, 1):
                    dve_moved, act_moved = groups_moved(0)
                    pe.wait_ge(xt_dve, dve_moved + 2)
                    pe.wait_ge(xt_act, act_moved + 2)
                elif (u, b) == (1, 2):
                    pe.wait_ge(embedded, n - 1)
                w = len(batch_tables(b)) * PAIR * P
                pe.matmul(id_row_bank(u, b)[:, 0:w], ones_r[:, :], diag[n % 2][:, 0:len(batch_tables(b)), :, :],
                          start=True, stop=True).then_inc(id_rows_ready, 1)

            def look_up(u, k):
                b = k // 2
                n = batch_of[u, b]
                out = bank_t[n % 2][:, (k % 2) * PAIR * P:(k % 2 + 1) * PAIR * P]
                pe.wait_ge(onehot_ready, K * u + batch_tables(b)[-1] + 1)
                if (u, k) == (0, 4):
                    pe.wait_ge(embedded, n - 1)
                if u == 0 and k < WHOLE:
                    pe.wait_ge(table_loaded[k], 16)
                    for c in range(RC):
                        mm = pe.matmul(out, raw[k][:, c * DIM:(c + 1) * DIM],
                                       onehot[n % 2].bitcast(F32)[:, k % 2, c, :], start=(c == 0), stop=(c == RC - 1))
                else:
                    if k >= WHOLE:
                        pe.wait_ge(hi_ready, split_place[k] + 1)
                    pe.wait_ge(lo_ready, split_place[k] + 1)
                    for c in range(RC):
                        for part, table in enumerate((table_hi, table_lo)):
                            mm = pe.matmul(out, table[k][:, c * DIM:(c + 1) * DIM], onehot[n % 2][:, k % 2, c, :],
                                           start=(c == 0 and part == 0), stop=(c == RC - 1 and part == 1))
                if k == batch_tables(b)[-1]:
                    mm.then_inc(looked_up, 1)

            def turn_group(t, g):
                if t == 2 and g < early_groups(t):
                    pe.wait_ge(embedded, 2 * BATCHES - 1 + g)
                if g in (2, 3) and g < early_groups(t):
                    pe.wait_ge((xt_dve, xt_act)[g % 2], groups_moved(t - 1)[g % 2] + 1)
                if t > 0 and g == 4:
                    pe.wait_ge(y_done, t)
                for n, s in enumerate(group_slots(g)):
                    if s < FEATURES:
                        pe.wait_ge(landed[t % 2][s], 16 * (t // 2) + 16)
                        rows = x[t % 2][:, s - K, :]
                    else:
                        pe.wait_ge(dense_loaded, 16)
                        rows = dense_sb[:, t, :]
                    mm = pe.transpose(group_bank(t, g)[:, n * P:(n + 1) * P], rows, ident[:, :])
                mm.then_inc(group_ready, 1)

            def grams(t):
                if t > 0:
                    pe.wait_ge(xt_dve, groups_moved(t)[0])
                pe.wait_ge(xt_act, groups_moved(t)[1])
                pe.wait_ge(embedded, BATCHES * (t // PAIR + 1))
                for q in range(QUADS):
                    if q >= 2:
                        if t + 1 == TILES:
                            pe.wait_ge(gram_dve, t + q - 1)
                        pe.wait_ge(gram_act, QUADS * t + q - 1)
                    for n in range(RQ):
                        p0 = S * (q * RQ + n)
                        at = SLOTS * S * (n % GROUP)
                        mm = pe.matmul(bank_g[q % 2][:, n // GROUP, at:at + SLOTS * S], xt[t % 2][:, p0:p0 + S, :],
                                       xt[t % 2][:, p0:p0 + S, 0:SLOTS], start=True, stop=True)
                    mm.then_inc(gram_ready, 1)

            def fold(t):
                pe.wait_ge(gram_dve, t + QUADS if t == TILES - 1 else t + 1)
                pe.wait_ge(gram_act, QUADS * t + QUADS)
                for i in range(NI):
                    g0, g1 = J * i, min(J * i + J, SLOTS)
                    mm = pe.transpose(bank_g[0][0:(g1 - g0) * R, i // GROUP, (i % GROUP) * P:(i % GROUP + 1) * P],
                                      gram[:, g0:g1, :], ident[:, :])
                    if i % GROUP == GROUP - 1 or i == NI - 1:
                        mm.then_inc(fold_ready, 1)

            def turn_pairs(t):
                pe.wait_ge(pairs_dve, t + 1)
                pe.wait_ge(pairs_act, t + 1)
                for s in range(S):
                    mm = pe.transpose(bank_g[1][0:PLACES, s // 2, (s % 2) * P:(s % 2 + 1) * P],
                                      pairs[:, s, :], ident[:, :])
                    if s % 2 == 1:
                        mm.then_inc(zt_ready, 1)

            def layer_1_dense(t):
                pe.wait_ge(dense_moved, t + 1)
                for n in range(C1):
                    pe.matmul(bank_m[n // 2][:, (n % 2) * P:(n % 2 + 1) * P], w1d_sb[:, n * P:(n + 1) * P],
                              dense_t[:, :, :], start=(n % 2 == 0), stop=False, skip_group_check=True)

            def layer_1_pairs(t):
                pe.wait_ge(zt_dve, t + 1)
                pe.wait_ge(zt_act, t + 1)
                for n in range(C1):
                    for j in range(J):
                        mm = pe.matmul(bank_m[n // 2][:, (n % 2) * P:(n % 2 + 1) * P], w1p_sb[:, j, n * P:(n + 1) * P],
                                       zt[:, :, j, :], start=False, stop=(j == J - 1), skip_group_check=True)
                    if n % 2 == 1:
                        mm.then_inc(h1_ready, 1)

            def layer_2(t):
                for n in range(C1):
                    if n == 0:
                        pe.wait_ge(h1_dve, t + 1)
                    if n == 2:
                        pe.wait_ge(h1_act, t + 1)
                    for m in range(C2):
                        mm = pe.matmul(bank_g[0][:, m, 0:P], w2_sb[:, n, m * P:(m + 1) * P], h1[:, n, :],
                                       start=(n == 0), stop=(n == C1 - 1))
                        if n == C1 - 1:
                            mm.then_inc(h2_ready, 1)

            def layer_3(t):
                pe.wait_ge(h2_dve, t + 1)
                pe.wait_ge(h2_act, t + 1)
                for m in range(C2):
                    mm = pe.matmul(bank_m[0][0:1, 0:P], w3_sb[:, m:m + 1], h2[:, m, :], start=(m == 0), stop=(m == C2 - 1))
                mm.then_inc(y_ready, 1)

            pe.wait_ge(const_ready, 3)
            pe.wait_ge(pads_ready, 3)
            id_rows(0, 0)
            id_rows(0, 1)
            for k in range(K):
                look_up(0, k)
                if k == 0:
                    id_rows(0, 2)
                turn_group(0, k)
            for g in range(K, GROUPS):
                turn_group(0, g)
            for t in range(TILES):
                early = t in (0, 2)
                if t > 0:
                    for g in range(early_groups(t), GROUPS):
                        turn_group(t, g)
                grams(t)
                if early:
                    turn_group(t + 1, 0)
                if t == 1:
                    look_up(1, 0)
                fold(t)
                if early:
                    turn_group(t + 1, 1)
                if t == 1:
                    look_up(1, 1)
                turn_pairs(t)
                if t == 1:
                    look_up(1, 2)
                if t == 0:
                    pe.wait_ge(weights_loaded, 16 * 6)
                layer_1_dense(t)
                if t == 1:
                    id_rows(1, 2)
                    look_up(1, 3)
                layer_1_pairs(t)
                if early:
                    turn_group(t + 1, 2)
                if t == 1:
                    look_up(1, 4)
                layer_2(t)
                if early:
                    turn_group(t + 1, 3)
                if t == 1:
                    turn_group(2, 0)
                    turn_group(2, 1)
                layer_3(t)
                if t == 0:
                    id_rows(1, 0)
                    id_rows(1, 1)

        def move_group(eng, eng_copy, done, t, g):
            slots = group_slots(g)
            n = len(slots)
            eng.wait_ge(group_ready, GROUPS * t + g + 1)
            move = eng_copy(xt[t % 2][:, :, slots[0]:slots[0] + n],
                            group_bank(t, g)[:, 0:n * P].rearrange("d (s p) -> d p s", p=P))
            move.then_inc(done, 1)
            if FEATURES in slots:
                eng_copy(dense_t[:, :, :],
                         group_bank(t, g)[:, (n - 1) * P:n * P].rearrange("d (r s) -> d s r", s=S)).then_inc(dense_moved, 1)

        def move_gram(eng_copy, q, s):
            rows = slice(FP * s, FP * s + FP)
            src = bank_g[q % 2][rows, :, 0:GROUP * S * SLOTS].rearrange("f b (r s g) -> f b r s g", r=GROUP, s=S)
            dst = gram[rows, :, q * RQ:(q + 1) * RQ].rearrange("f g (b r) -> f b r g", b=2)
            return eng_copy(dst, src[:, :, :, s, :])

        def dve_takes_part(t, q):
            return q == QUADS - 1 or t == TILES - 1

        def move_pairs(eng_copy, b):
            i0, i1 = GROUP * b, min(GROUP * b + GROUP, NI)
            for i in range(max(i0, 1), i1):
                np_ = (min(J * i + J, SLOTS) - J * i) * R
                src = bank_g[0][0:np_, b, (i - i0) * P:(i - i0 + 1) * P].rearrange("p (s f) -> p s f", s=S)
                eng_copy(pairs[0:np_, :, RECT[i]:RECT[i + 1]], src[:, :, 0:J * i])
            for j in range(1, J):
                n = (i1 if J * (i1 - 1) + j < SLOTS else i1 - 1) - i0
                rows = slice(R * j, R * j + R)
                src = bank_g[0][rows, b, 0:BANK].rearrange("p (i s f) -> p i s f", i=GROUP, s=S)
                dst = pairs[rows, :, RECT[NI]:].rearrange("p s (i f) -> p i s f", f=J - 1)
                for f in range(j):
                    start = J * i0 + f
                    last = eng_copy(dst[:, i0:i0 + n, :, f],
                                    diagonal(bank_g[0], rows, b, start, n))
            return last

        def diagonal(bank, rows, b, start, n):
            flat = bank[rows, b, :]
            ap = bass.AP(flat.tensor, flat.offset + start, [list(flat.ap[0]), [P + J, n], [FP, S]])
            return ap

        @block.vector
        def _(dve):
            def copy(o, i):
                return dve.tensor_copy(o, i)

            def make_diag(u, b):
                n, ks = batch_of[u, b], batch_tables(b)
                if n >= 2:
                    dve.wait_ge(id_rows_ready, n - 1)
                for i, k in enumerate(ks):
                    last = dve.tensor_tensor(diag[n % 2][:, i, :, :], ident[:, None, :].to_broadcast([P, PAIR, P]),
                                             ids_f[:, PAIR * u:PAIR * u + PAIR, k:k + 1].to_broadcast([P, PAIR, P]),
                                             ALU.mult)
                last.then_inc(diag_ready, 1)

            def make_onehots(u, b):
                n = batch_of[u, b]
                dve.wait_ge(id_rows_ready, n + 1)
                if n >= 2:
                    dve.wait_ge(looked_up, n - 1)
                for i in range(len(batch_tables(b))):
                    dve.tensor_tensor(onehot[n % 2][:, i, :, :],
                                      id_row_bank(u, b)[0:RP, None, i * PAIR * P:(i + 1) * PAIR * P].to_broadcast([RP, RC, PAIR * P]),
                                      row_id[0:RP, :, None].to_broadcast([RP, RC, PAIR * P]),
                                      ALU.is_equal).then_inc(onehot_ready, 1)

            dve.memset(ones[:, :], 1.0).then_inc(ones_ready, 1)
            dve.wait_ge(ones_ready, 1)
            dve.tensor_copy(ones_r[:, :], ones[:, :]).then_inc(const_ready, 1)
            for b in range(2):
                dve.memset(xt[b][:, :, SLOTS:], 0.0).then_inc(pads_ready, 1)
            dve.memset(pairs[:, :, :], 0.0).then_inc(pads_ready, 1)
            dve.wait_ge(ids_loaded, 16)
            for k, f in enumerate(ONEHOT):
                dve.tensor_copy(ids_f[:, :, k:k + 1], ids_sb[:, :, f:f + 1]).then_inc(ids_f_ready, 1)
            dve.wait_ge(ids_f_ready, K)
            dve.wait_ge(const_ready, 3)
            def split_table(k):
                n = split_place[k]
                dve.wait_ge(table_loaded[k], 16)
                if 2 <= n < K - WHOLE + 2:
                    dve.wait_ge(hi_ready, n - 1)
                dve.tensor_scalar(upper[n % 2].bitcast(U32)[:, :], raw[k].bitcast(U32)[:, :], HIGH_BITS, None,
                                  ALU.bitwise_and).then_inc(upper_ready, 1)
                dve.wait_ge(upper_ready, n + 1)
                if k < WHOLE:
                    dve.tensor_copy(table_hi[k][:, :], upper[n % 2][:, :])
                dve.tensor_tensor(table_lo[k][:, :], raw[k][:, :], upper[n % 2][:, :], ALU.subtract).then_inc(lo_ready, 1)

            make_diag(0, 0)
            make_diag(0, 1)
            make_onehots(0, 0)
            make_diag(0, 2)
            make_onehots(0, 1)
            split_table(2)
            split_table(3)
            make_onehots(0, 2)
            split_table(4)
            for t in range(TILES):
                for g in dve_groups(t):
                    if g >= early_groups(t):
                        move_group(dve, copy, xt_dve, t, g)
                if t == 0:
                    make_diag(1, 0)
                    make_diag(1, 1)
                    for k in range(WHOLE):
                        split_table(k)
                for q in range(QUADS):
                    if dve_takes_part(t, q):
                        dve.wait_ge(gram_ready, QUADS * t + q + 1)
                        move_gram(copy, q, 0)
                        move_gram(copy, q, 1).then_inc(gram_dve, 1)
                if t in (0, 2):
                    move_group(dve, copy, xt_dve, t + 1, 0)
                dve.wait_ge(fold_ready, 2 * t + 1)
                move_pairs(copy, 0).then_inc(pairs_dve, 1)
                dve.wait_ge(zt_ready, 2 * t + 1)
                dve.tensor_copy(zt[:, 0:2, :, :], bank_g[1][0:PLACES, 0, 0:2 * P]).then_inc(zt_dve, 1)
                if t == 1:
                    make_diag(1, 2)
                    make_onehots(1, 2)
                if t == 0:
                    dve.wait_ge(weights_loaded, 16 * 6)
                dve.wait_ge(h1_ready, 2 * t + 1)
                for n in range(2):
                    last = dve.tensor_scalar(h1[:, n, :], bank_m[0][:, n * P:(n + 1) * P], b1_sb[:, n:n + 1], 0.0,
                                             ALU.add, ALU.max)
                last.then_inc(h1_dve, 1)
                if t in (0, 2):
                    move_group(dve, copy, xt_dve, t + 1, 2)
                dve.wait_ge(h2_ready, 2 * t + 1)
                dve.tensor_scalar(h2[:, 0, :], bank_g[0][:, 0, 0:P], b2_sb[:, 0:1], 0.0, ALU.add, ALU.max).then_inc(h2_dve, 1)
                if t == 1:
                    move_group(dve, copy, xt_dve, 2, 0)
                dve.wait_ge(y_ready, t + 1)
                dve.tensor_copy(y_row.rearrange("o (r s t) -> o t s r", s=S, t=TILES)[:, t, :, :],
                                bank_m[0][0:1, 0:P].rearrange("o (s r) -> o s r", s=S)).then_inc(y_done, 1)
                if t == 0:
                    make_onehots(1, 0)
                    make_onehots(1, 1)

        @block.scalar
        def _(act):
            def copy(o, i):
                return act.copy(o, i)

            act.dma_start(dense_sb[:, :, :], dense_tiles).then_inc(dense_loaded, 16)
            act.dma_start(w1p_sb[:, :, :], w1_pairs).then_inc(weights_loaded, 16)
            act.dma_start(w1d_sb[:, :], w1_dense).then_inc(weights_loaded, 16)
            act.dma_start(w2_sb[:, :, :], w2.rearrange("(c p) n -> p c n", p=P)).then_inc(weights_loaded, 16)
            act.dma_start(w3_sb[:, :], w3).then_inc(weights_loaded, 16)
            act.dma_start(b1_sb[:, :], b1).then_inc(weights_loaded, 16)
            act.dma_start(b2_sb[:, :], b2).then_inc(weights_loaded, 16)
            def move_look_ups(u, b):
                n, ks = batch_of[u, b], batch_tables(b)
                act.wait_ge(looked_up, n + 1)
                for i in range(PAIR):
                    src = bank_t[n % 2][:, 0:len(ks) * PAIR * P].rearrange("d (k i p) -> d i p k", i=PAIR, p=P)
                    last = act.copy(xt[i][:, :, ks[0]:ks[0] + len(ks)], src[:, i, :, :])
                last.then_inc(embedded, 1)

            def copy_upper(n):
                act.wait_ge(upper_ready, n + 1)
                act.copy(table_hi[SPLIT[n]][:, :], upper[n % 2][:, :]).then_inc(hi_ready, 1)

            act.wait_ge(pads_ready, 3)
            copy_upper(0)
            for g in range(GROUPS):
                if 1 <= g < K - WHOLE:
                    copy_upper(g)
                if g < K and g == batch_tables(g // 2)[-1]:
                    move_look_ups(0, g // 2)
                move_group(act, copy, xt_act, 0, g)
            act.wait_ge(weights_loaded, 16 * 6)
            for t in range(TILES):
                if t > 0:
                    for g in range(GROUPS):
                        if g not in dve_groups(t) and g >= early_groups(t):
                            move_group(act, copy, xt_act, t, g)
                for q in range(QUADS):
                    act.wait_ge(gram_ready, QUADS * t + q + 1)
                    for s in (range(2, S) if dve_takes_part(t, q) else range(S)):
                        last = move_gram(copy, q, s)
                    last.then_inc(gram_act, 1)
                act.wait_ge(fold_ready, 2 * t + 2)
                move_pairs(copy, 1).then_inc(pairs_act, 1)
                act.wait_ge(zt_ready, 2 * t + 2)
                act.copy(zt[:, 2:4, :, :], bank_g[1][0:PLACES, 1, 0:2 * P]).then_inc(zt_act, 1)
                if t in (0, 2):
                    move_group(act, copy, xt_act, t + 1, 1)
                if t == 1:
                    move_look_ups(1, 0)
                    move_look_ups(1, 1)
                act.wait_ge(h1_ready, 2 * t + 2)
                for n in range(2, 4):
                    last = act.activation(h1[:, n, :], bank_m[1][:, (n - 2) * P:(n - 1) * P], ACT.Relu, bias=b1_sb[:, n:n + 1])
                last.then_inc(h1_act, 1)
                if t == 1:
                    move_look_ups(1, 2)
                act.wait_ge(h2_ready, 2 * t + 2)
                act.activation(h2[:, 1, :], bank_g[0][:, 1, 0:P], ACT.Relu, bias=b2_sb[:, 1:2]).then_inc(h2_act, 1)
                if t in (0, 2):
                    move_group(act, copy, xt_act, t + 1, 3)
                if t == 1:
                    move_group(act, copy, xt_act, 2, 1)


def kernel(**inputs):
    import numpy as np
    import concourse.bacc as bacc
    from concourse.bass_utils import run_bass_kernel_spmd

    w1 = np.asarray(inputs["W_top1"])
    n_pairs = SLOTS * (SLOTS - 1) // 2
    w1_pairs = np.zeros((PLACES, J, N1), w1.dtype)
    for place, j, f, g in pair_places():
        a, b = sorted((SLOT_OF[f], SLOT_OF[g]))
        w1_pairs[place, j] = w1[a * SLOTS - a * (a + 1) // 2 + b - a - 1]
    data = {
        "dense": np.asarray(inputs["r_dense_x"]),
        "ids": np.asarray(inputs["ids"]),
        "w1_pairs": w1_pairs,
        "w1_dense": w1[n_pairs:],
        "b1": np.asarray(inputs["b_top1"]).reshape(C1, P).T,
        "w2": np.asarray(inputs["W_top2"]),
        "b2": np.asarray(inputs["b_top2"]).reshape(C2, P).T,
        "w3": np.asarray(inputs["W_top3"]).reshape(C2, P).T,
    }
    for f in range(FEATURES):
        data[f"table_{f}"] = np.asarray(inputs[f"tbl_{f}"])

    nc = bacc.Bacc("TRN2", target_bir_lowering=False, num_devices=1)
    arrays, aps = {}, {}
    for name, a in data.items():
        arrays[f"in_{name}"] = np.ascontiguousarray(a)
        aps[name] = nc.dram_tensor(f"in_{name}", a.shape, mybir.dt.from_np(a.dtype), kind="ExternalInput").ap()
    out = nc.dram_tensor("out_y", (BATCH, 1), F32, kind="ExternalOutput").ap()
    dlrm_tower(nc, aps["dense"], aps["ids"], [aps[f"table_{f}"] for f in range(FEATURES)], aps["w1_pairs"],
               aps["w1_dense"], aps["b1"], aps["w2"], aps["b2"], aps["w3"], out)
    r = run_bass_kernel_spmd(nc, [arrays], core_ids=[0])
    return r.results[0]["out_y"]
```

```python
from contextlib import ExitStack

import concourse.bass as bass
from concourse import mybir

F32 = mybir.dt.float32
I32 = mybir.dt.int32
U32 = mybir.dt.uint32
F32R = mybir.dt.float32r
HIGH_BITS = 0xFFFFF000
ALU = mybir.AluOpType
ACT = mybir.ActivationFunctionType

P = 128
BATCH = 512
TILES = BATCH // P
FEATURES = 26
DIM = 128
SLOTS = FEATURES + 1
N1, N2 = 512, 256
C1, C2 = N1 // P, N2 // P

ONEHOT = [1, 8, 9, 10, 18, 19]
ROWS = 1000
RP = 125
RC = ROWS // RP
K = len(ONEHOT)
GATHERED = [f for f in range(FEATURES) if f not in ONEHOT]
SLOT_OF = ONEHOT + GATHERED + [FEATURES]

GROUP = 4
GROUPS = -(-(SLOTS - K) // GROUP)
PAIR = 2
BATCHES = -(-K // 2)
WHOLE = 3
SPLIT = [*range(WHOLE, K), *range(WHOLE)]
S = 4
R = P // S
FP = 32
QUADS = 4
RQ = R // QUADS
J = 4
NI = -(-SLOTS // J)
RECT = [2 * i * (i - 1) for i in range(NI + 1)]
PLACES = RECT[NI] + (J - 1) * NI
BANK = 512


def pair_places():
    for g in range(SLOTS):
        i, j = divmod(g, J)
        for f in range(g):
            place = RECT[i] + f if f < J * i else RECT[NI] + (J - 1) * i + f - J * i
            yield place, j, f, g


def dlrm_tower(nc, dense, ids, onehot_ids, tables, w1_pairs, w1_dense, b1, w2, b2, w3, out):
    with ExitStack() as ctx:
        def sb(name, shape, dt=F32):
            return ctx.enter_context(nc.sbuf_tensor(name, shape, dt))

        def sem(name):
            return ctx.enter_context(nc.semaphore(name))

        ones = sb("ones", [P, P])
        ident = sb("ident", [P, P])
        row_id = sb("row_id", [P, RC])
        raw = [sb(f"raw{i}", [RP, RC * DIM]) for i in range(WHOLE + 2)]
        raw = [raw[k if k < WHOLE else WHOLE + k % 2] for k in range(K)]
        upper = [sb(f"upper{i}", [RP, RC * DIM]) for i in range(2)]
        table_hi = [sb(f"table_hi{k}", [RP, RC * DIM], F32R) for k in range(K)]
        table_lo = [sb(f"table_lo{k}", [RP, RC * DIM], F32R) for k in range(K)]
        w1p_sb = sb("w1p_sb", [PLACES, J, N1])
        w1d_sb = sb("w1d_sb", [DIM, N1])
        w2_sb = sb("w2_sb", [P, C1, N2])
        w3_sb = sb("w3_sb", [P, C2])
        b1_sb = sb("b1_sb", [P, C1])
        b2_sb = sb("b2_sb", [P, C2])
        ids_sb = sb("ids_sb", [P, TILES, FEATURES], I32)
        id_rows = sb("id_rows", [RP, K, TILES * P], I32)
        onehot = [sb(f"onehot{b}", [RP, 2, RC, PAIR * P], F32R) for b in range(2)]
        dense_sb = sb("dense_sb", [P, TILES, DIM])
        x = [sb(f"x{b}", [P, FEATURES - K, DIM]) for b in range(2)]
        xt = [sb(f"xt{b}", [P, P, FP]) for b in range(2)]
        ahead = sb("ahead", [P, P, 2])
        dense_t = sb("dense_t", [P, S, R])
        gram = sb("gram", [P, SLOTS, R])
        pairs = sb("pairs", [P, S, PLACES])
        zt = sb("zt", [PLACES, S, J, R])
        h1 = sb("h1", [P, C1, P])
        h2 = sb("h2", [P, C2, P])
        y_row = sb("y_row", [1, BATCH])

        bank_t = [ctx.enter_context(nc.psum_tensor(f"bank_t{i}", [P, BANK], F32)) for i in range(2)]
        bank_g = [ctx.enter_context(nc.psum_tensor(f"bank_g{i}", [P, 2, BANK], F32)) for i in range(2)]
        bank_m = [ctx.enter_context(nc.psum_tensor(f"bank_m{i}", [P, BANK], F32)) for i in range(2)]

        dense_loaded = sem("dense_loaded")
        ids_loaded = sem("ids_loaded")
        table_loaded = [sem(f"table_loaded{k}") for k in range(K)]
        upper_ready = sem("upper_ready")
        hi_ready = sem("hi_ready")
        lo_ready = sem("lo_ready")
        weights_loaded = sem("weights_loaded")
        landed = [{s: sem(f"landed{b}_{s}") for s in range(K, FEATURES)} for b in range(2)]
        ones_ready = sem("ones_ready")
        const_ready = sem("const_ready")
        pads_ready = sem("pads_ready")
        id_rows_loaded = [sem(f"id_rows_loaded{i}") for i in range(3)]
        onehot_ready = sem("onehot_ready")
        looked_up = sem("looked_up")
        embedded = sem("embedded")
        ahead_moved = sem("ahead_moved")
        group_ready = sem("group_ready")
        dense_moved = sem("dense_moved")
        xt_dve, xt_act = sem("xt_dve"), sem("xt_act")
        gram_ready = sem("gram_ready")
        gram_half_ready = sem("gram_half_ready")
        gram_dve, gram_act = sem("gram_dve"), sem("gram_act")
        fold_ready = sem("fold_ready")
        pairs_dve, pairs_act = sem("pairs_dve"), sem("pairs_act")
        zt_ready = sem("zt_ready")
        zt_dve, zt_act = sem("zt_dve"), sem("zt_act")
        h1_ready = sem("h1_ready")
        h1_dve, h1_act = sem("h1_dve"), sem("h1_act")
        h2_ready = sem("h2_ready")
        h2_dve, h2_act = sem("h2_dve"), sem("h2_act")
        y_ready = sem("y_ready")
        y_done = sem("y_done")
        stored = sem("stored")

        ids_tiles = ids.rearrange("(p t) f -> p t f", t=TILES)
        dense_tiles = dense.rearrange("(p t) d -> p t d", t=TILES)

        def group_slots(g):
            return range(K + GROUP * g, min(K + GROUP * g + GROUP, SLOTS))

        def early_groups(t):
            return (0, 2, 2, GROUPS)[t]

        def group_bank(t, g):
            if g < early_groups(t):
                return (bank_t[g % 2] if g < 5 else bank_m[1])[:, :]
            return (bank_g[0][:, 0, :], bank_g[0][:, 1, :], bank_g[1][:, 0, :], bank_g[1][:, 1, :],
                    bank_m[1][:, :], bank_t[0][:, :])[g]

        def dve_groups(t):
            return range(4, 5) if t == 0 else range(0, GROUPS, 2)

        def groups_moved(t):
            by_dve = sum(len(dve_groups(i)) for i in range(t + 1))
            return by_dve, GROUPS * (t + 1) - by_dve

        def groups_after(k):
            first = 0 if k == 0 else groups_after(k - 1).stop
            return range(first, GROUPS if k == K - 1 else max(first, min(GROUPS, (0, 0, 1, 2, 3, 3, 5, 5)[k + 1])))

        def id_rows_part(u, k):
            return 2 if u else 0 if k < 2 else 1

        def batch_tables(b):
            return range(2 * b, min(2 * b + 2, K))

        split_place = {k: n for n, k in enumerate(SPLIT)}

        batches = [(u, b) for u in range(TILES // PAIR) for b in range(BATCHES)]
        batch_of = {ub: n for n, ub in enumerate(batches)}

        def load_id_rows(eng, u, ks):
            rows = onehot_ids[ks[0]:ks[-1] + 1, u * PAIR * P:(u + 1) * PAIR * P]
            eng.dma_start(id_rows[:, ks[0]:ks[-1] + 1, u * PAIR * P:(u + 1) * PAIR * P],
                          bass.AP(rows.tensor, rows.offset, [[0, RP], *[list(d) for d in rows.ap]])
                          ).then_inc(id_rows_loaded[id_rows_part(u, ks[0])], 16)

        block = ctx.enter_context(nc.Block())

        @block.sync
        def _(sp):
            sp.dma_start(ids_sb[:, :, :], ids_tiles).then_inc(ids_loaded, 16)
            for k, f in enumerate(ONEHOT):
                if k == 1:
                    load_id_rows(sp, 0, range(2, K))
                if k >= WHOLE + 2:
                    sp.wait_ge(lo_ready, split_place[k - 2] + 1)
                sp.dma_start(raw[k][:, :], tables[f].rearrange("(p c) d -> p (c d)", c=RC)).then_inc(table_loaded[k], 16)
            sp.dma_start(w1p_sb[:, :, :], w1_pairs).then_inc(weights_loaded, 16)
            sp.dma_start(w1d_sb[:, :], w1_dense).then_inc(weights_loaded, 16)
            sp.dma_start(w2_sb[:, :, :], w2.rearrange("(c p) n -> p c n", p=P)).then_inc(weights_loaded, 16)
            sp.dma_start(w3_sb[:, :], w3).then_inc(weights_loaded, 16)
            sp.dma_start(b1_sb[:, :], b1).then_inc(weights_loaded, 16)
            sp.dma_start(b2_sb[:, :], b2).then_inc(weights_loaded, 16)
            load_id_rows(sp, 1, range(K))
            sp.wait_ge(y_done, TILES)
            sp.dma_start(out.rearrange("b o -> o b"), y_row[:, :]).then_inc(stored, 16)
            sp.wait_ge(stored, 16)

        @block.gpsimd
        def _(pool):
            pool.iota(row_id[:, :], [[1, RC]], base=0, channel_multiplier=RC,
                      allow_small_or_imprecise_dtypes=True).then_inc(const_ready, 1)
            pool.wait_ge(ones_ready, 1)
            pool.affine_select(out=ident[:, :], in_=ones[:, :], compare_op=ALU.is_equal, fill=0.0, base=0,
                               pattern=[[-1, P]], channel_multiplier=1).then_inc(const_ready, 1)
            pool.wait_ge(ids_loaded, 16)
            for t in range(TILES):
                for g in range(GROUPS):
                    if t >= 2:
                        pool.wait_ge(group_ready, GROUPS * (t - 2) + g + 1)
                    for s in group_slots(g):
                        if s < FEATURES:
                            f = SLOT_OF[s]
                            pool.indirect_dma_start(
                                x[t % 2][:, s - K, :], None, tables[f][:, :],
                                bass.IndirectOffsetOnAxis(ap=ids_sb[:, t, f:f + 1], axis=0)).then_inc(landed[t % 2][s], 16)

        @block.tensor
        def _(pe):
            def look_up(u, k):
                b = k // 2
                n = batch_of[u, b]
                out = bank_t[n % 2][:, (k % 2) * PAIR * P:(k % 2 + 1) * PAIR * P]
                if (u, k) != (0, 0):
                    pe.wait_ge(onehot_ready, RC * (K * u + (k if (u, b) == (0, 0) else batch_tables(b)[-1]) + 1))
                if k == batch_tables(b)[0] and n >= 2:
                    pe.wait_ge(embedded, n - 1)
                if k == batch_tables(b)[0] and u == 1 and b > 0:
                    pe.wait_ge(xt_dve, groups_moved(1)[0])
                    pe.wait_ge(xt_act, groups_moved(1)[1])
                if u == 0 and k < WHOLE:
                    pe.wait_ge(table_loaded[k], 16)
                    for c in range(RC):
                        if k == 0:
                            pe.wait_ge(onehot_ready, c + 1)
                        mm = pe.matmul(out, raw[k][:, c * DIM:(c + 1) * DIM],
                                       onehot[n % 2].bitcast(F32)[:, k % 2, c, :], start=(c == 0), stop=(c == RC - 1))
                else:
                    if k >= WHOLE:
                        pe.wait_ge(hi_ready, split_place[k] + 1)
                    pe.wait_ge(lo_ready, split_place[k] + 1)
                    for c in range(RC):
                        for part, table in enumerate((table_hi, table_lo)):
                            mm = pe.matmul(out, table[k][:, c * DIM:(c + 1) * DIM], onehot[n % 2][:, k % 2, c, :],
                                           start=(c == 0 and part == 0), stop=(c == RC - 1 and part == 1))
                if k == batch_tables(b)[-1]:
                    mm.then_inc(looked_up, 1)

            def turn_group(t, g):
                if (t, g) == (1, 1):
                    pe.wait_ge(embedded, BATCHES + 1)
                if t == 2 and g < early_groups(t):
                    pe.wait_ge(embedded, 2 * BATCHES - 1 + g)
                if 2 <= g < min(5, early_groups(t)):
                    pe.wait_ge((xt_dve, xt_act)[g % 2], groups_moved(t - 1)[g % 2] + g // 2)
                if t in (1, 2) and g == 5:
                    pe.wait_ge(xt_dve, groups_moved(t - 1)[0] + 1)
                if t == 0 and g == 5:
                    pe.wait_ge(embedded, BATCHES)
                for n, s in enumerate(group_slots(g)):
                    if s < FEATURES:
                        pe.wait_ge(landed[t % 2][s], 16 * (t // 2) + 16)
                        rows = x[t % 2][:, s - K, :]
                    else:
                        pe.wait_ge(dense_loaded, 16)
                        rows = dense_sb[:, t, :]
                    mm = pe.transpose(group_bank(t, g)[:, n * P:(n + 1) * P], rows, ident[:, :])
                mm.then_inc(group_ready, 1)

            def grams(t):
                pe.wait_ge(xt_dve, groups_moved(t)[0])
                pe.wait_ge(xt_act, groups_moved(t)[1])
                pe.wait_ge(embedded, BATCHES * (t // PAIR + 1))
                if t == 3:
                    pe.wait_ge(ahead_moved, 1)
                for q in range(QUADS):
                    if q >= 2:
                        if t + 1 == TILES:
                            pe.wait_ge(gram_dve, t + q - 1)
                        pe.wait_ge(gram_act, QUADS * t + q - 1)
                    for n in range(RQ):
                        p0 = S * (q * RQ + n)
                        at = SLOTS * S * (n % GROUP)
                        mm = pe.matmul(bank_g[q % 2][0:FP * (S - 1) + SLOTS, n // GROUP, at:at + SLOTS * S],
                                       xt[t % 2].rearrange("d p f -> d (p f)")[:, FP * p0:FP * (p0 + S - 1) + SLOTS],
                                       xt[t % 2][:, p0:p0 + S, 0:SLOTS], start=True, stop=True)
                        if q == QUADS - 1 and n == GROUP - 1:
                            mm.then_inc(gram_half_ready, 1)
                    mm.then_inc(gram_ready, 1)

            def fold(t):
                pe.wait_ge(gram_dve, t + QUADS if t == TILES - 1 else t + 1)
                pe.wait_ge(gram_act, QUADS * t + QUADS)
                for i in range(NI):
                    g0, g1 = J * i, min(J * i + J, SLOTS)
                    mm = pe.transpose(bank_g[0][0:(g1 - g0) * R, i // GROUP, (i % GROUP) * P:(i % GROUP + 1) * P],
                                      gram[:, g0:g1, :], ident[:, :])
                    if i % GROUP == GROUP - 1 or i == NI - 1:
                        mm.then_inc(fold_ready, 1)

            def turn_pairs(t):
                pe.wait_ge(pairs_dve, t + 1)
                pe.wait_ge(pairs_act, t + 1)
                for s in range(S):
                    mm = pe.transpose(bank_g[1][0:PLACES, s // 2, (s % 2) * P:(s % 2 + 1) * P],
                                      pairs[:, s, :], ident[:, :])
                    if s % 2 == 1:
                        mm.then_inc(zt_ready, 1)

            def layer_1_dense(t, chunks):
                if t == 0:
                    pe.wait_ge(weights_loaded, 16 * 6)
                pe.wait_ge(dense_moved, t + 1)
                for n in chunks:
                    pe.matmul(bank_m[n // 2][:, (n % 2) * P:(n % 2 + 1) * P], w1d_sb[:, n * P:(n + 1) * P],
                              dense_t[:, :, :], start=(n % 2 == 0), stop=False, skip_group_check=True)

            def early_chunks(t):
                return (0, 0, 1, 2)[t]

            def layer_1_pairs(t):
                pe.wait_ge(zt_dve, t + 1)
                pe.wait_ge(zt_act, t + 1)
                for n in range(C1):
                    for j in range(J):
                        mm = pe.matmul(bank_m[n // 2][:, (n % 2) * P:(n % 2 + 1) * P], w1p_sb[:, j, n * P:(n + 1) * P],
                                       zt[:, :, j, :], start=False, stop=(j == J - 1), skip_group_check=True)
                    if n % 2 == 1:
                        mm.then_inc(h1_ready, 1)

            def layer_2(t):
                for n, m in ((0, 0), (0, 1), (1, 0), (1, 1), (2, 0), (3, 0), (2, 1), (3, 1)):
                    if (n, m) == (0, 0):
                        pe.wait_ge(h1_dve, t + 1)
                    if (n, m) == (2, 0):
                        pe.wait_ge(h1_act, t + 1)
                    mm = pe.matmul(bank_g[0][:, m, 0:P], w2_sb[:, n, m * P:(m + 1) * P], h1[:, n, :],
                                   start=(n == 0), stop=(n == C1 - 1))
                    if n == C1 - 1:
                        mm.then_inc(h2_ready, 1)

            def layer_3(t):
                for m in range(C2):
                    pe.wait_ge((h2_dve, h2_act)[m], t + 1)
                    mm = pe.matmul(bank_m[0][0:1, 0:P], w3_sb[:, m:m + 1], h2[:, m, :], start=(m == 0), stop=(m == C2 - 1))
                mm.then_inc(y_ready, 1)

            pe.wait_ge(const_ready, 2)
            pe.wait_ge(pads_ready, 4)
            for k in range(K):
                look_up(0, k)
                for g in groups_after(k):
                    turn_group(0, g)
            for t in range(TILES):
                grams(t)
                if t < 2:
                    look_up(1, 2 * t)
                if t == 2:
                    turn_group(3, 0)
                fold(t)
                if t < 2:
                    look_up(1, 2 * t + 1)
                if t == 2:
                    turn_group(3, 1)
                layer_1_dense(t, range(early_chunks(t)))
                turn_pairs(t)
                if t == 1:
                    look_up(1, 4)
                layer_1_dense(t, range(early_chunks(t), C1))
                layer_1_pairs(t)
                if t == 1:
                    for k in range(5, K):
                        look_up(1, k)
                if t < 2:
                    turn_group(t + 1, 0)
                if t == 2:
                    turn_group(3, 2)
                layer_2(t)
                if t < 2:
                    for g in range(1, GROUPS):
                        turn_group(t + 1, g)
                if t == 2:
                    for g in range(3, GROUPS):
                        turn_group(3, g)
                layer_3(t)

        def move_group(eng, eng_copy, done, t, g):
            slots = group_slots(g)
            n = len(slots)
            eng.wait_ge(group_ready, GROUPS * t + g + 1)
            move = eng_copy(xt[t % 2][:, :, slots[0]:slots[0] + n],
                            group_bank(t, g)[:, 0:n * P].rearrange("d (s p) -> d p s", p=P))
            move.then_inc(done, 1)
            if FEATURES in slots:
                eng_copy(dense_t[:, :, :],
                         group_bank(t, g)[:, (n - 1) * P:n * P].rearrange("d (r s) -> d s r", s=S)).then_inc(dense_moved, 1)

        def move_gram(eng_copy, q, s, banks=range(2)):
            rows = slice(FP * s, FP * s + SLOTS)
            src = bank_g[q % 2][rows, banks[0]:banks[-1] + 1, 0:GROUP * S * SLOTS].rearrange("f b (r s g) -> f b r s g", r=GROUP, s=S)
            r0 = q * RQ + GROUP * banks[0]
            dst = gram[rows, :, r0:r0 + GROUP * len(banks)].rearrange("f g (b r) -> f b r g", b=len(banks))
            return eng_copy(dst, src[:, :, :, s, :])

        def move_last_grams(eng, eng_copy, t, quadrants):
            for bank, ready, count in ((0, gram_half_ready, t + 1), (1, gram_ready, QUADS * t + QUADS)):
                eng.wait_ge(ready, count)
                for s in quadrants:
                    last = move_gram(eng_copy, QUADS - 1, s, range(bank, bank + 1))
            return last

        def dve_takes_part(t, q):
            return q == QUADS - 1 or t == TILES - 1

        def move_pairs(eng_copy, b):
            i0, i1 = GROUP * b, min(GROUP * b + GROUP, NI)
            for i in range(max(i0, 1), i1):
                np_ = (min(J * i + J, SLOTS) - J * i) * R
                src = bank_g[0][0:np_, b, (i - i0) * P:(i - i0 + 1) * P].rearrange("p (s f) -> p s f", s=S)
                eng_copy(pairs[0:np_, :, RECT[i]:RECT[i + 1]], src[:, :, 0:J * i])
            for j in range(1, J):
                n = (i1 if J * (i1 - 1) + j < SLOTS else i1 - 1) - i0
                rows = slice(R * j, R * j + R)
                src = bank_g[0][rows, b, 0:BANK].rearrange("p (i s f) -> p i s f", i=GROUP, s=S)
                dst = pairs[rows, :, RECT[NI]:].rearrange("p s (i f) -> p i s f", f=J - 1)
                last = eng_copy(dst[:, i0:i0 + n, :, 0:j], diagonal(bank_g[0], rows, b, J * i0, n, j))
            return last

        def diagonal(bank, rows, b, start, n, width):
            flat = bank[rows, b, :]
            ap = bass.AP(flat.tensor, flat.offset + start, [list(flat.ap[0]), [P + J, n], [FP, S], [1, width]])
            return ap

        @block.vector
        def _(dve):
            def copy(o, i):
                return dve.tensor_copy(o, i)

            def make_onehots(u, ks):
                n, i = batch_of[u, ks[0] // 2], ks[0] % 2
                dve.wait_ge(id_rows_loaded[id_rows_part(u, ks[0])], 16)
                if n >= 2:
                    dve.wait_ge(looked_up, n - 1)
                for c in range(RC):
                    dve.tensor_scalar(onehot[n % 2][:, i:i + len(ks), c, :],
                                      id_rows[:, ks[0]:ks[0] + len(ks), u * PAIR * P:(u + 1) * PAIR * P],
                                      row_id[0:RP, c:c + 1], None, ALU.is_equal).then_inc(onehot_ready, len(ks))

            def split_table(k):
                n = split_place[k]
                dve.wait_ge(table_loaded[k], 16)
                if 2 <= n < K - WHOLE + 2:
                    dve.wait_ge(hi_ready, n - 1)
                dve.tensor_scalar(upper[n % 2].bitcast(U32)[:, :], raw[k].bitcast(U32)[:, :], HIGH_BITS, None,
                                  ALU.bitwise_and).then_inc(upper_ready, 1)
                dve.wait_ge(upper_ready, n + 1)
                if k < WHOLE:
                    dve.tensor_copy(table_hi[k][:, :], upper[n % 2][:, :])
                dve.tensor_tensor(table_lo[k][:, :], raw[k][:, :], upper[n % 2][:, :], ALU.subtract).then_inc(lo_ready, 1)

            dve.memset(ones[:, :], 1.0).then_inc(ones_ready, 1)
            for b in range(2):
                dve.memset(xt[b][:, :, SLOTS:], 0.0).then_inc(pads_ready, 1)
            dve.memset(pairs[:, :, :], 0.0).then_inc(pads_ready, 1)
            dve.memset(gram[:, :, :], 0.0).then_inc(pads_ready, 1)
            dve.wait_ge(const_ready, 1)
            for k in batch_tables(0):
                make_onehots(0, [k])
            for b in range(1, BATCHES):
                for i, k in enumerate(batch_tables(b)):
                    if i == 1:
                        make_onehots(0, batch_tables(b))
                    if k >= WHOLE:
                        split_table(k)
            for t in range(TILES):
                if t == 0:
                    for k in range(WHOLE):
                        if k == WHOLE - 1:
                            for g in dve_groups(0):
                                move_group(dve, copy, xt_dve, 0, g)
                        split_table(k)
                    make_onehots(1, batch_tables(0))
                if t == 1:
                    for b in range(1, BATCHES):
                        make_onehots(1, batch_tables(b))
                for q in range(QUADS - 1):
                    if dve_takes_part(t, q):
                        dve.wait_ge(gram_ready, QUADS * t + q + 1)
                        move_gram(copy, q, 0)
                        move_gram(copy, q, 1).then_inc(gram_dve, 1)
                move_last_grams(dve, copy, t, range(2)).then_inc(gram_dve, 1)
                if t == 1:
                    dve.wait_ge(embedded, BATCHES + 1)
                    dve.tensor_copy(xt[1][:, :, 0:2], ahead[:, :, :]).then_inc(ahead_moved, 1)
                if t == 2:
                    move_group(dve, copy, xt_dve, t + 1, 0)
                dve.wait_ge(fold_ready, 2 * t + 1)
                move_pairs(copy, 0).then_inc(pairs_dve, 1)
                dve.wait_ge(zt_ready, 2 * t + 1)
                dve.tensor_copy(zt[:, 0:2, :, :], bank_g[1][0:PLACES, 0, 0:2 * P]).then_inc(zt_dve, 1)
                if t == 0:
                    dve.wait_ge(weights_loaded, 16 * 6)
                dve.wait_ge(h1_ready, 2 * t + 1)
                for n in range(2):
                    last = dve.tensor_scalar(h1[:, n, :], bank_m[0][:, n * P:(n + 1) * P], b1_sb[:, n:n + 1], 0.0,
                                             ALU.add, ALU.max)
                last.then_inc(h1_dve, 1)
                if t < 3:
                    move_group(dve, copy, xt_dve, t + 1, 2 if t == 2 else 0)
                dve.wait_ge(h2_ready, 2 * t + 1)
                dve.tensor_scalar(h2[:, 0, :], bank_g[0][:, 0, 0:P], b2_sb[:, 0:1], 0.0, ALU.add, ALU.max).then_inc(h2_dve, 1)
                for g in (range(2, GROUPS, 2) if t < 2 else range(4, GROUPS, 2) if t == 2 else ()):
                    move_group(dve, copy, xt_dve, t + 1, g)
                dve.wait_ge(y_ready, t + 1)
                dve.tensor_copy(y_row.rearrange("o (r s t) -> o t s r", s=S, t=TILES)[:, t, :, :],
                                bank_m[0][0:1, 0:P].rearrange("o (s r) -> o s r", s=S)).then_inc(y_done, 1)

        @block.scalar
        def _(act):
            def copy(o, i):
                return act.copy(o, i)

            def move_look_ups(u, b):
                n, ks = batch_of[u, b], batch_tables(b)
                act.wait_ge(looked_up, n + 1)
                for i in range(PAIR):
                    src = bank_t[n % 2][:, 0:len(ks) * PAIR * P].rearrange("d (k i p) -> d i p k", i=PAIR, p=P)
                    to = ahead if (u, b, i) == (1, 0, 1) else xt[i][:, :, ks[0]:ks[0] + len(ks)]
                    last = act.copy(to[:, :, :], src[:, i, :, :])
                last.then_inc(embedded, 1)

            def copy_upper(n):
                act.wait_ge(upper_ready, n + 1)
                act.copy(table_hi[SPLIT[n]][:, :], upper[n % 2][:, :]).then_inc(hi_ready, 1)

            load_id_rows(act, 0, batch_tables(0))
            act.dma_start(dense_sb[:, :, :], dense_tiles).then_inc(dense_loaded, 16)
            act.wait_ge(pads_ready, 4)
            copy_upper(0)
            for k in range(K):
                if 1 <= k < K - WHOLE:
                    copy_upper(k)
                if k == batch_tables(k // 2)[-1]:
                    move_look_ups(0, k // 2)
                for g in groups_after(k):
                    if g not in dve_groups(0):
                        move_group(act, copy, xt_act, 0, g)
            act.wait_ge(weights_loaded, 16 * 6)
            for t in range(TILES):
                for q in range(QUADS - 1):
                    act.wait_ge(gram_ready, QUADS * t + q + 1)
                    for s in (range(2, S) if dve_takes_part(t, q) else range(S)):
                        last = move_gram(copy, q, s)
                    last.then_inc(gram_act, 1)
                move_last_grams(act, copy, t, range(2, S)).then_inc(gram_act, 1)
                act.wait_ge(fold_ready, 2 * t + 2)
                move_pairs(copy, 1).then_inc(pairs_act, 1)
                act.wait_ge(zt_ready, 2 * t + 2)
                act.copy(zt[:, 2:4, :, :], bank_g[1][0:PLACES, 1, 0:2 * P]).then_inc(zt_act, 1)
                if t == 2:
                    move_group(act, copy, xt_act, t + 1, 1)
                if t < 2:
                    move_look_ups(1, t)
                act.wait_ge(h1_ready, 2 * t + 2)
                for n in range(2, 4):
                    last = act.activation(h1[:, n, :], bank_m[1][:, (n - 2) * P:(n - 1) * P], ACT.Relu, bias=b1_sb[:, n:n + 1])
                last.then_inc(h1_act, 1)
                if t == 1:
                    move_look_ups(1, 2)
                act.wait_ge(h2_ready, 2 * t + 2)
                act.activation(h2[:, 1, :], bank_g[0][:, 1, 0:P], ACT.Relu, bias=b2_sb[:, 1:2]).then_inc(h2_act, 1)
                for g in (range(1, GROUPS, 2) if t < 2 else range(3, GROUPS, 2) if t == 2 else ()):
                    move_group(act, copy, xt_act, t + 1, g)


def kernel(**inputs):
    import numpy as np
    import concourse.bacc as bacc
    from concourse.bass_utils import run_bass_kernel_spmd

    w1 = np.asarray(inputs["W_top1"])
    n_pairs = SLOTS * (SLOTS - 1) // 2
    w1_pairs = np.zeros((PLACES, J, N1), w1.dtype)
    for place, j, f, g in pair_places():
        a, b = sorted((SLOT_OF[f], SLOT_OF[g]))
        w1_pairs[place, j] = w1[a * SLOTS - a * (a + 1) // 2 + b - a - 1]
    data = {
        "dense": np.asarray(inputs["r_dense_x"]),
        "ids": np.asarray(inputs["ids"]),
        "onehot_ids": np.asarray(inputs["ids"])[:, ONEHOT].T.reshape(K, P, TILES).transpose(0, 2, 1).reshape(K, TILES * P),
        "w1_pairs": w1_pairs,
        "w1_dense": w1[n_pairs:],
        "b1": np.asarray(inputs["b_top1"]).reshape(C1, P).T,
        "w2": np.asarray(inputs["W_top2"]),
        "b2": np.asarray(inputs["b_top2"]).reshape(C2, P).T,
        "w3": np.asarray(inputs["W_top3"]).reshape(C2, P).T,
    }
    for f in range(FEATURES):
        data[f"table_{f}"] = np.asarray(inputs[f"tbl_{f}"])

    nc = bacc.Bacc("TRN2", target_bir_lowering=False, num_devices=1)
    arrays, aps = {}, {}
    for name, a in data.items():
        arrays[f"in_{name}"] = np.ascontiguousarray(a)
        aps[name] = nc.dram_tensor(f"in_{name}", a.shape, mybir.dt.from_np(a.dtype), kind="ExternalInput").ap()
    out = nc.dram_tensor("out_y", (BATCH, 1), F32, kind="ExternalOutput").ap()
    dlrm_tower(nc, aps["dense"], aps["ids"], aps["onehot_ids"], [aps[f"table_{f}"] for f in range(FEATURES)], aps["w1_pairs"],
               aps["w1_dense"], aps["b1"], aps["w2"], aps["b2"], aps["w3"], out)
    r = run_bass_kernel_spmd(nc, [arrays], core_ids=[0])
    return r.results[0]["out_y"]
```
